# Optimizing a Trainium2 kernel written in Bass

```python
import numpy as np
import jax
import jax.numpy as jnp

def _softmax(x, axis=-1):
    return jax.nn.softmax(x, axis=axis)

def _gelu(x):
    return jax.nn.gelu(x, approximate=True)

def _silu(x):
    return jax.nn.silu(x)

def _sigmoid(x):
    return jax.nn.sigmoid(x)

def _layernorm(x, axis=-1, eps=1e-05):
    m = jnp.mean(x, axis=axis, keepdims=True)
    v = jnp.var(x, axis=axis, keepdims=True)
    return (x - m) / jnp.sqrt(v + eps)

def _scatter_add(tgt, idx, src, axis=0):
    return tgt.at[idx].add(src)

def _segment_sum(src, seg, n):
    return jax.ops.segment_sum(src, seg, n)
kernel_name = 'mk_adj_resnorm_d1_adj_r2_fc2b85'

def setup_inputs(seed: int=0):
    np.random.seed(seed)
    _w = jnp.asarray

    def _rec_inputs():
        import jax
        import jax.numpy as jnp
        _gk = jax.random.key(seed)
        x = -0.000929 + 1 * jax.random.normal(jax.random.fold_in(_gk, 1), (8192, 128), jnp.float32)
        _a = jax.random.bernoulli(jax.random.fold_in(_gk, 2), 0.000488281, (8192, 8192))
        _a = jnp.logical_or(_a, jnp.eye(8192, dtype=bool))
        _af = _a.astype(jnp.float32)
        _af = _af * jax.random.uniform(jax.random.fold_in(_gk, 3), (8192, 8192), jnp.float32, 0.05, 1)
        adj = _af
        return (x, adj)
    x, adj = _rec_inputs()

    def _L0_gnn_setup():
        import jax, jax.numpy as jnp
        import numpy as np
        N, D = (4096, 128)
        key = jax.random.key(seed)
        k1, k2 = jax.random.split(key)
        h = jax.random.normal(k1, (N, D), dtype=jnp.float32)
        adj = jax.random.uniform(k2, (N, N), dtype=jnp.float32)
        I = jnp.eye(N, dtype=jnp.float32)
        lambda_ = jnp.array(1.0, dtype=jnp.float32)
        return {'h': h, 'adj': adj, 'I': I, 'lambda_': lambda_}
    _L0_gnn_all = _L0_gnn_setup()
    _L0_gnn_in = {k: v for k, v in _L0_gnn_all.items() if k in ('lambda_',)}
    del _L0_gnn_all
    return {'x': x, 'adj': adj, 'L0_gnn_lambda_': _L0_gnn_in['lambda_']}

def reference(x, adj, L0_gnn_lambda_):
    import jax
    import jax.numpy as jnp

    def _L0_gnn_ref(h, adj, I, lambda_):
        import jax, jax.numpy as jnp
        import numpy as np
        N, D = (4096, 128)
        lambda_max = 1.0 + jax.nn.relu(lambda_)
        alpha = (2.0 * lambda_max - 2.0) / lambda_max
        beta = 2.0 / lambda_max
        Ak = alpha * I + beta * adj
        row_sum = Ak.sum(axis=1)
        d_inv_sqrt = jnp.power(row_sum, -0.5)
        d_inv_sqrt = jnp.where(jnp.isinf(d_inv_sqrt), 0.0, d_inv_sqrt)
        A = d_inv_sqrt[:, None] * Ak * d_inv_sqrt[None, :]
        return A @ h
    eye = jnp.eye(8192, dtype=adj.dtype)
    x = _layernorm(x + _L0_gnn_ref(x, adj, eye, L0_gnn_lambda_), axis=-1)
    return x

_drawn_inputs = setup_inputs


def setup_inputs(seed=0):
    import zlib

    import numpy as np

    out = dict(_drawn_inputs(seed))
    spreads = {}
    factors = {}
    for name, (base, spread) in spreads.items():
        noise = np.random.default_rng([zlib.crc32(name.encode()), seed]).standard_normal(out[name].shape)
        drawn = base * np.exp(spread * noise) if base else spread * noise
        out[name] = jnp.asarray(drawn.astype(out[name].dtype))
    for name, factor in factors.items():
        out[name] = (out[name] * factor).astype(out[name].dtype)
    return out
```

```python
from contextlib import ExitStack

import concourse.bass as bass
from concourse import mybir

ALU = mybir.AluOpType
ACT = mybir.ActivationFunctionType
AX = mybir.AxisListType
F32 = mybir.dt.float32

P = 128
K = 4
W = P * K
D = 128
EPS = 1e-5

BAND = 3
RING = 6
LANES = 4
BANKS = 4
TURN_LAG = 2
MIXED = 4
SUMS = 2


def gnn_resnorm(nc, x, adj, lam, out):
    N = x.shape[0]
    NP = N // W
    LAST = NP - 1

    adj_rows = adj.rearrange("c r p f -> (c r p) f")
    x_rows = x.rearrange("(r p k) d -> (r p) (k d)", p=P, k=K)
    out_rows = out.rearrange("(r p k) d -> (r p) (k d)", p=P, k=K)

    class Step:
        def __init__(self, t, before):
            self.t = t
            self.held = [t] + [r for r in range(t - BAND, t) if r >= 0] if t >= 0 else []
            self.pairs = max(0, LAST - (t + 1 + BAND))
            self.tail = LAST - t - self.pairs
            self.again = max(0, t - BAND)
            self.width = 2 if t >= 0 else 1
            if before is None:
                self.load0 = self.ring0 = self.prod0 = self.sum0 = 0
            else:
                self.load0, self.ring0, self.prod0, self.sum0 = before.ends
            w, cols = self.width, self.width - 1
            self.load_tail = self.load0 + w * self.pairs
            self.ring_tail = self.ring0 + w * self.pairs
            self.load_again = self.load_tail + w * self.tail
            self.ring_again = self.ring_tail + cols * self.tail
            self.prod_pairs = self.prod0 + len(self.held)
            self.prod_tail = self.prod_pairs + cols * self.pairs
            self.prod_again = self.prod_tail + cols * self.tail
            self.sum_tail = self.sum0 + w * self.pairs
            self.sum_end = self.sum_tail + w * self.tail
            self.ends = (self.load_again + self.again, self.ring_again + self.again,
                         self.prod_again + self.again, self.sum_end)
            self.after_row = min(2, self.again) if t < LAST else 0

    steps = []
    for t in range(-1, NP):
        steps.append(Step(t, steps[-1] if steps else None))
    final = steps[-1]

    def repeat(eng, count, unroll, body, first=0, apart=0):
        for s in range(first, first + apart):
            body(s, s, 0)
        first, count = first + apart, count - apart
        full = count // unroll
        if full >= 2:
            with eng.Fori(0, full) as i:
                for j in range(unroll):
                    body(i * unroll + (first + j), first + j, i)
        else:
            full = 0
        for s in range(first + full * unroll, first + count):
            body(s, s, 0)

    with ExitStack() as ctx:
        def sb(name, shape):
            return ctx.enter_context(nc.sbuf_tensor(name, shape, F32))

        def ps(name, shape):
            return ctx.enter_context(nc.psum_tensor(name, shape, F32))

        def sem(name):
            return ctx.enter_context(nc.semaphore(name))

        acc = sb("acc", [P, NP * W])
        part = sb("part", [P, NP * W])
        ring = sb("ring", [P, RING * K * W])
        held = sb("held", [P, (BAND + 1) * (BAND + 2) // 2 * K * W])
        block_sum = sb("block_sum", [P, SUMS * W])
        xin = sb("xin", [P, 2, W])
        y = sb("y", [P, 2, W])
        ones = sb("ones", [P, 1])
        neg_half = sb("neg_half", [P, K])
        ident = sb("ident", [P, P])
        lam_sb = sb("lam_sb", [P, 1])
        coef = sb("coef", [P, 8])
        alpha, beta = coef[:, 4:5], coef[:, 3:4]
        rs = sb("rs", [P, 5, K])
        d_all = sb("d_all", [P, NP * K])
        d_sq = sb("d_sq", [P, NP * K])
        own = sb("own", [P, NP * K])
        nbr = sb("nbr", [P, NP * K])
        stats = sb("stats", [P, 2, K, 6])
        mv = sb("mv", [P, 2, K, 2])
        rstd = sb("rstd", [P, 2, K])
        var_eps = sb("var_eps", [P, 2, K])
        shift = sb("shift", [P, 2, K])
        nmean = sb("nmean", [P, 2, K])

        prod = ps("prod", [P, BANKS * 512])
        row_ps = ps("row_ps", [P, 512])
        turned = ps("turned", [P, 2, 512])

        lane = [sem(f"load_lane{j}") for j in range(LANES)]
        ring_free = sem("ring_free")
        summed = sem("summed")
        part_added = sem("part_added")
        multiplied = sem("multiplied")
        gathered = sem("gathered")
        row_summed = sem("row_summed")
        pow_asked = sem("pow_asked")
        pow_done = sem("pow_done")
        y_ready = sem("y_ready")
        x_loaded = [sem(f"x_loaded{j}") for j in range(2)]
        lam_loaded = sem("lam_loaded")
        pool_set = sem("pool_set")
        ident_set = sem("ident_set")
        dve_chain = sem("dve_chain")
        pool_chain = sem("pool_chain")
        scales_ready = sem("scales_ready")
        xe_loaded = [sem(f"xe_loaded{j}") for j in range(2)]
        transposed = sem("transposed")
        nbr_scaled = sem("nbr_scaled")
        own_scaled = sem("own_scaled")
        stats_done = sem("stats_done")
        norm_ready = sem("norm_ready")
        normed = sem("normed")
        stored = [sem(f"stored{j}") for j in range(2)]

        def slot(q):
            return ring[:, bass.ds((q % RING) * (K * W), K * W)]

        def held_slot(r, c):
            d = c - r
            s = d * (d + 1) // 2 + c % (d + 1)
            return held[:, s * K * W:(s + 1) * K * W]

        def adj_block(c, r):
            return adj_rows[bass.ds((c * NP + r) * P, P), :]

        def bank(m):
            return prod[:, bass.ds((m % BANKS) * 512, 512)]

        def sum_buf(e):
            return block_sum[:, bass.ds((e % SUMS) * W, W)]

        def panel(t, r):
            return t[:, bass.ds(r * W, W)]

        def wait_load(eng, base, per, unroll, i, extra=0):
            value = base // LANES + 1 + extra + i * (per * unroll // LANES)
            if not isinstance(value, int) or value > 0:
                eng.wait_ge(lane[base % LANES], value * 16)

        def pair_unroll(w):
            return LANES // w

        def epilogue_rows():
            return final.held + list(range(final.again))

        def result(e):
            return out_buf[:, (e % 2) * W:(e % 2 + 1) * W]

        out_buf = held[:, 0:2 * W]
        own_x = held[:, 2 * W:4 * W]
        mixed = held[:, 4 * W:(4 + MIXED) * W]

        block = ctx.enter_context(nc.Block())

        @block.sync
        def _(sp):
            sp.dma_start(lam_sb[:, :], lam[0:1, 0:1].to_broadcast([P, 1])).then_inc(lam_loaded, 16)

            def load(dst, src, n, per, unroll, i):
                wait_load(sp, n, per, unroll, i, extra=-1)
                sp.dma_start(dst, src).then_inc(lane[n % LANES], 16)

            def load_ring(q, qbase, src, n, per, unroll, i):
                if qbase >= RING:
                    sp.wait_ge(ring_free, q - (RING - 1))
                load(slot(q), src, n, per, unroll, i)

            for st in steps:
                t, w = st.t, st.width
                u = pair_unroll(w)

                def pair(s, base, i):
                    n, q = st.load0 + w * base, st.ring0 + w * s
                    qb = st.ring0 + w * base
                    load_ring(q, qb, adj_block(LAST - s, t + 1), n, w, u, i)
                    if t >= 0:
                        load_ring(q + 1, qb + 1, adj_block(t, s + (t + 1)), n + 1, w, u, i)

                repeat(sp, st.pairs, u, pair, apart=RING if t < 0 else 0)
                for s in range(st.tail):
                    n, q = st.load_tail + w * s, st.ring_tail + s
                    c = LAST - st.pairs - s
                    if t >= 0 and s == 0:
                        sp.wait_ge(multiplied, st.prod_pairs)
                    load(held_slot(t + 1, c), adj_block(c, t + 1), n, 0, 0, 0)
                    if t >= 0:
                        load_ring(q, q, adj_block(t, t + 1 + st.pairs + s), n + 1, 0, 0, 0)

                def again(s, base, i):
                    load_ring(st.ring_again + s, st.ring_again + base, adj_block(t, s),
                              st.load_again + base, 1, LANES, i)

                repeat(sp, st.again, LANES, again)

        @block.tensor
        def _(pe):
            def product(rhs, m, mbase, t):
                if mbase >= BANKS:
                    pe.wait_ge(gathered, m - (BANKS - 1))
                for k in range(K):
                    mm = pe.matmul(bank(m), y[:, t % 2, k * D:(k + 1) * D], rhs[:, k * W:(k + 1) * W],
                                   start=(k == 0), stop=(k == K - 1))
                mm.then_inc(multiplied, 1)

            def row_sums(r, sums):
                pe.wait_ge(part_added, sums)
                for k in range(K):
                    mm = pe.matmul(row_ps[:, k:k + 1], part[:, r * W + k:(r + 1) * W:K], ones[:, :],
                                   start=True, stop=True)
                mm.then_inc(row_summed, 1)

            def turn(e):
                r = epilogue_rows()[e]
                pe.wait_ge(gathered, final.prod0 + e + 1)
                if e == 0:
                    pe.wait_ge(ident_set, 1)
                if e >= 2:
                    pe.wait_ge(nbr_scaled, e - 1)
                for k in range(K):
                    mm = pe.transpose(turned[:, e % 2, k * P:(k + 1) * P],
                                      acc[:, r * W + k:(r + 1) * W:K], ident[:, :])
                mm.then_inc(transposed, 1)

            pe.wait_ge(pool_set, 1)
            for st in steps:
                t, w = st.t, st.width
                u = pair_unroll(w)
                if t >= 0:
                    pe.wait_ge(y_ready, t + 1)
                    for j, r in enumerate(st.held):
                        product(held_slot(r, t), st.prod0 + j, st.prod0 + j, t)

                    def pair(s, base, i):
                        wait_load(pe, st.load0 + w * base + 1, w, u, i)
                        product(slot(st.ring0 + 1 + w * s), st.prod_pairs + s, st.prod_pairs + base, t)

                    repeat(pe, st.pairs, u, pair, apart=BANKS - 1 if t == 0 else 0)
                    for s in range(st.tail):
                        wait_load(pe, st.load_tail + w * s + 1, 0, 0, 0)
                        product(slot(st.ring_tail + s), st.prod_tail + s, st.prod_tail + s, t)

                if t == LAST:
                    break

                def again(s, base, i):
                    wait_load(pe, st.load_again + base, 1, LANES, i)
                    product(slot(st.ring_again + s), st.prod_again + s, st.prod_again + base, t)

                repeat(pe, st.again - st.after_row, LANES, again)
                row_sums(t + 1, st.sum_end)
                repeat(pe, st.after_row, LANES, again, first=st.again - st.after_row)

            for e in range(NP + TURN_LAG):
                if len(final.held) <= e < NP:
                    s = e - len(final.held)
                    wait_load(pe, final.load_again + s, 0, 0, 0)
                    product(slot(final.ring_again + s), final.prod0 + e, final.prod0 + e, LAST)
                if e >= len(final.held):
                    for f in range(e - TURN_LAG if e > len(final.held) else 0, e - TURN_LAG + 1):
                        turn(f)

        @block.vector
        def _(dve):
            link_count = [0]

            def link(ins):
                link_count[0] += 1
                ins.then_inc(dve_chain, 1)
                dve.wait_ge(dve_chain, link_count[0])

            link(nc.vector.memset(ones[:, :], 1.0))
            dve.wait_ge(lam_loaded, 16)
            link(nc.vector.tensor_scalar(coef[:, 0:1], lam_sb[:, :], 0.0, 1.0, ALU.max, ALU.add))
            link(nc.vector.reciprocal(coef[:, 1:2], coef[:, 0:1]))
            link(nc.vector.tensor_scalar(coef[:, 2:3], coef[:, 0:1], 2.0, -2.0, ALU.mult, ALU.add))
            link(nc.vector.tensor_scalar(beta, coef[:, 1:2], 2.0, None, ALU.mult))
            link(nc.vector.tensor_tensor(alpha, coef[:, 2:3], coef[:, 1:2], ALU.mult))
            dve.wait_ge(pool_set, 1)

            def block_sums(src, e, ebase, done=None):
                if ebase >= SUMS:
                    dve.wait_ge(part_added, e - (SUMS - 1))
                nc.vector.tensor_reduce(sum_buf(e), src.rearrange("p (k i) -> p i k", k=K), AX.X,
                                        ALU.add).then_inc(summed, 1)

            def free_slots(sums, count):
                dve.wait_ge(summed, sums)
                dve.sem_inc(ring_free, count)

            def gather(m, r):
                nc.vector.tensor_tensor(panel(acc, r), panel(acc, r), bank(m), ALU.add).then_inc(gathered, 1)

            def scale_x(r):
                dve.wait_ge(row_summed, r + 1)
                link(nc.vector.tensor_scalar(rs[:, 0, :], row_ps[:, 0:K], beta, alpha, ALU.mult, ALU.add))
                link(nc.vector.tensor_scalar(rs[:, 1, :], rs[:, 0, :], 0.0, None, ALU.is_equal))
                nc.vector.tensor_tensor(rs[:, 2, :], rs[:, 0, :], rs[:, 1, :], ALU.add).then_inc(pow_asked, 1)
                link(nc.vector.tensor_scalar(rs[:, 3, :], rs[:, 1, :], -1.0, 1.0, ALU.mult, ALU.add))
                dve.wait_ge(pow_done, r + 1)
                d = d_all[:, r * K:(r + 1) * K]
                link(nc.vector.tensor_tensor(d, rs[:, 4, :], rs[:, 3, :], ALU.mult))
                dve.wait_ge(x_loaded[r % 2], 16 * (r // 2 + 1))
                nc.vector.tensor_tensor(y[:, r % 2, :].rearrange("p (k d) -> p k d", k=K),
                                        xin[:, r % 2, :].rearrange("p (k d) -> p k d", k=K),
                                        d.unsqueeze(2).to_broadcast([P, K, D]), ALU.mult).then_inc(y_ready, 1)

            for st in steps[:-1]:
                t, w = st.t, st.width
                u = pair_unroll(w)
                for j, r in enumerate(st.held):
                    dve.wait_ge(multiplied, st.prod0 + j + 1)
                    gather(st.prod0 + j, r)

                def pair(s, base, i):
                    n, q, e = st.load0 + w * base, st.ring0 + w * s, st.sum0 + w * s
                    eb = st.sum0 + w * base
                    wait_load(dve, n, w, u, i)
                    block_sums(slot(q), e, eb)
                    if t >= 0:
                        wait_load(dve, n + 1, w, u, i)
                        block_sums(slot(q + 1), e + 1, eb + 1)
                        dve.wait_ge(multiplied, st.prod_pairs + s + 1)
                        free_slots(e + 2, 2)
                        gather(st.prod_pairs + s, s + (t + 1))
                    else:
                        free_slots(e + 1, 1)

                repeat(dve, st.pairs, u, pair, apart=SUMS if t < 0 else 0)
                for s in range(st.tail):
                    n, q, e = st.load_tail + w * s, st.ring_tail + s, st.sum_tail + w * s
                    c = LAST - st.pairs - s
                    wait_load(dve, n, 0, 0, 0)
                    block_sums(held_slot(t + 1, c), e, e)
                    if t >= 0:
                        wait_load(dve, n + 1, 0, 0, 0)
                        block_sums(slot(q), e + 1, e + 1)
                        dve.wait_ge(multiplied, st.prod_tail + s + 1)
                        free_slots(e + 2, 1)
                        gather(st.prod_tail + s, t + 1 + st.pairs + s)

                def again(s, base, i):
                    dve.wait_ge(multiplied, st.prod_again + s + 1)
                    dve.sem_inc(ring_free, 1)
                    gather(st.prod_again + s, s)

                repeat(dve, st.again - st.after_row, LANES, again)
                scale_x(t + 1)
                repeat(dve, st.after_row, LANES, again, first=st.again - st.after_row)

            dve.wait_ge(y_ready, NP)
            nc.vector.tensor_scalar(nbr[:, :], d_all[:, :], beta, None, ALU.mult)
            link(nc.vector.tensor_tensor(d_sq[:, :], d_all[:, :], d_all[:, :], ALU.mult))
            nc.vector.tensor_scalar(own[:, :], d_sq[:, :], alpha, 1.0, ALU.mult, ALU.add).then_inc(scales_ready, 1)

            def panel_stats(e):
                b = e % 2
                dve.wait_ge(nbr_scaled, e + 1)
                dve.wait_ge(own_scaled, e + 1)
                if e >= 2:
                    dve.wait_ge(norm_ready, e - 1)
                m = mixed[:, e % MIXED * W:(e % MIXED + 1) * W]
                link(nc.vector.tensor_tensor(m, m, own_x[:, b * W:(b + 1) * W], ALU.add))
                for k in range(K):
                    ins = nc.vector.bn_stats(stats[:, b, k, :], m[:, k * D:(k + 1) * D])
                link(ins)
                for k in range(K):
                    ins = nc.vector.bn_aggr(mv[:, b, k, :], stats[:, b, k, :])
                ins.then_inc(stats_done, 1)

            lag = TURN_LAG + 1
            for e in range(NP + lag):
                if e < NP:
                    dve.wait_ge(multiplied, final.prod0 + e + 1)
                    if e >= len(final.held):
                        dve.sem_inc(ring_free, 1)
                    gather(final.prod0 + e, epilogue_rows()[e])
                if e >= lag:
                    panel_stats(e - lag)

        @block.gpsimd
        def _(pool):
            link_count = [0]

            def link(ins):
                link_count[0] += 1
                ins.then_inc(pool_chain, 1)
                pool.wait_ge(pool_chain, link_count[0])

            nc.gpsimd.memset(part[:, :], 0.0)
            nc.gpsimd.memset(neg_half[:, :], -0.5)
            link(nc.gpsimd.memset(ident[:, :], 0.0))
            nc.gpsimd.affine_select(out=ident[:, :], in_=ident[:, :], compare_op=ALU.not_equal, fill=1.0,
                                    base=0, pattern=[[-1, P]], channel_multiplier=1).then_inc(ident_set, 1)
            nc.gpsimd.memset(acc[:, :], 0.0).then_inc(pool_set, 1)
            pool.wait_ge(pool_set, 1)

            def add_sums(e, ebase, r):
                pool.wait_ge(summed, e + 1)
                if ebase >= 1:
                    pool.wait_ge(part_added, e)
                nc.gpsimd.tensor_tensor(panel(part, r), panel(part, r), sum_buf(e),
                                        ALU.add).then_inc(part_added, 1)

            for st in steps[:-1]:
                t, w = st.t, st.width

                def pair(s, base, i):
                    e = st.sum0 + w * s
                    add_sums(e, st.sum0 + w * base, t + 1)
                    if t >= 0:
                        add_sums(e + 1, st.sum0 + w * base + 1, s + (t + 1))

                repeat(pool, st.pairs + st.tail, 2, pair, apart=1 if t < 0 else 0)
                pool.wait_ge(pow_asked, t + 2)
                nc.gpsimd.tensor_tensor(rs[:, 4, :], rs[:, 2, :], neg_half[:, :], ALU.pow).then_inc(pow_done, 1)

            def norm_scales(e):
                b = e % 2
                pool.wait_ge(stats_done, e + 1)
                if e >= 2:
                    pool.wait_ge(normed, e - 1)
                nc.gpsimd.tensor_scalar(nmean[:, b, :], mv[:, b, :, 0], -1.0, None, ALU.mult)
                link(nc.gpsimd.tensor_scalar(var_eps[:, b, :], mv[:, b, :, 1], EPS, None, ALU.add))
                link(nc.gpsimd.tensor_tensor(rstd[:, b, :], var_eps[:, b, :], neg_half[:, :], ALU.pow))
                nc.gpsimd.tensor_tensor(shift[:, b, :], nmean[:, b, :], rstd[:, b, :],
                                        ALU.mult).then_inc(norm_ready, 1)

            pool.wait_ge(scales_ready, 1)
            pool.wait_ge(multiplied, final.prod_pairs)
            for e in range(NP + 1):
                if e < NP:
                    r, b = epilogue_rows()[e], e % 2
                    pool.wait_ge(xe_loaded[b], 16 * (e // 2 + 1))
                    if e >= 2:
                        pool.wait_ge(stats_done, e - 1)
                    nc.gpsimd.tensor_tensor(
                        own_x[:, b * W:(b + 1) * W].rearrange("p (k d) -> p k d", k=K),
                        xin[:, b, :].rearrange("p (k d) -> p k d", k=K),
                        own[:, r * K:(r + 1) * K].unsqueeze(2).to_broadcast([P, K, D]),
                        ALU.mult).then_inc(own_scaled, 1)
                if e >= 1:
                    norm_scales(e - 1)

        @block.scalar
        def _(act):
            for r in range(NP):
                if r >= 2:
                    act.wait_ge(y_ready, r - 1)
                act.dma_start(xin[:, r % 2, :], x_rows[r * P:(r + 1) * P, :]).then_inc(x_loaded[r % 2], 16)

            def load_x(e):
                r = epilogue_rows()[e]
                if e >= 2:
                    act.wait_ge(own_scaled, e - 1)
                act.dma_start(xin[:, e % 2, :], x_rows[r * P:(r + 1) * P, :]).then_inc(xe_loaded[e % 2], 16)

            act.wait_ge(scales_ready, 1)
            load_x(0)
            act.wait_ge(multiplied, final.prod_pairs)
            for e in range(NP + 2):
                if e + 1 < NP:
                    load_x(e + 1)
                if e < NP:
                    r, b = epilogue_rows()[e], e % 2
                    act.wait_ge(transposed, e + 1)
                    m0 = e % MIXED * W
                    if e >= MIXED:
                        act.wait_ge(stats_done, e - MIXED + 1)
                    for k in range(K):
                        ins = nc.scalar.activation(mixed[:, m0 + k * D:m0 + (k + 1) * D],
                                                   turned[:, b, k * P:(k + 1) * P], ACT.Copy,
                                                   scale=nbr[:, r * K + k:r * K + k + 1])
                    ins.then_inc(nbr_scaled, 1)
                if e >= 2:
                    f, b = e - 2, e % 2
                    m0 = f % MIXED * W
                    act.wait_ge(norm_ready, f + 1)
                    if f >= 2:
                        act.wait_ge(stored[b], 16 * (f // 2))
                    for k in range(K):
                        ins = nc.scalar.activation(result(f)[:, k * D:(k + 1) * D],
                                                   mixed[:, m0 + k * D:m0 + (k + 1) * D], ACT.Identity,
                                                   bias=shift[:, b, k:k + 1], scale=rstd[:, b, k:k + 1])
                    ins.then_inc(normed, 1)
                    r = epilogue_rows()[f]
                    act.wait_ge(normed, f + 1)
                    act.dma_start(out_rows[r * P:(r + 1) * P, :], result(f)).then_inc(stored[b], 16)
            for j in range(2):
                act.wait_ge(stored[j], 16 * (NP // 2))


def kernel(x, adj, L0_gnn_lambda_):
    import numpy as np
    import concourse.bacc as bacc
    from concourse.bass_utils import run_bass_kernel_spmd

    x, adj, lam = np.asarray(x), np.asarray(adj), np.asarray(L0_gnn_lambda_)
    NP = x.shape[0] // W
    blocks = adj.reshape(NP, W, NP, P, K).transpose(2, 0, 3, 4, 1).reshape(NP, NP, P, K * W)
    arrays = {"x_dram": np.ascontiguousarray(x), "adj_dram": np.ascontiguousarray(blocks),
              "lam_dram": np.ascontiguousarray(lam.reshape(1, 1))}
    nc = bacc.Bacc("TRN2", target_bir_lowering=False, num_devices=1)
    args = [nc.dram_tensor(n, a.shape, mybir.dt.from_np(a.dtype), kind="ExternalInput").ap()
            for n, a in arrays.items()]
    out = nc.dram_tensor("out_dram", x.shape, F32, kind="ExternalOutput").ap()
    gnn_resnorm(nc, *args, out)
    r = run_bass_kernel_spmd(nc, [arrays], core_ids=[0])
    return r.results[0]["out_dram"]
```

```python
from contextlib import ExitStack

import concourse.bass as bass
from concourse import mybir

ALU = mybir.AluOpType
ACT = mybir.ActivationFunctionType
AX = mybir.AxisListType
F32 = mybir.dt.float32

P = 128
K = 4
W = P * K
D = 128
EPS = 1e-5

BAND = 3
RING = 6
LANES = 4
BANKS = 4
TURN_LAG = 2
HELD_LAG = 3
ROW_AT = 1
BEFORE_ROW = 2
MIXED = 4
SUMS = 2


def gnn_resnorm(nc, x, adj, lam, out):
    N = x.shape[0]
    NP = N // W
    LAST = NP - 1

    adj_rows = adj.rearrange("c r p f -> (c r p) f")
    x_rows = x.rearrange("(r p k) d -> (r p) (k d)", p=P, k=K)
    out_rows = out.rearrange("(r p k) d -> (r p) (k d)", p=P, k=K)

    class Step:
        def __init__(self, t, before):
            self.t = t
            self.held = [r for r in range(t - BAND, t + 1) if r >= 0] if t >= 0 else []
            self.pairs = max(0, LAST - (t + 1 + BAND))
            self.tail = LAST - t - self.pairs
            self.again = max(0, t - BAND)
            self.width = 2 if t >= 0 else 1
            if before is None:
                self.ring0 = self.prod0 = self.sum0 = 0
            else:
                self.ring0, self.prod0, self.sum0 = before.ends
            w, cols = self.width, self.width - 1
            self.between = min(self.pairs, len(self.held))
            front = len(self.held) - self.between
            self.held_prod = [self.prod0 + j + max(0, j - front + 1) for j in range(len(self.held))]
            self.ring_tail = self.ring0 + w * self.pairs
            self.ring_again = self.ring_tail + cols * self.tail
            self.lag = HELD_LAG if t >= 0 else 1
            self.early = min(self.tail, max(0, self.pairs - self.lag))
            self.row_early = t >= 0 and self.early == self.tail
            self.prod_pairs = self.prod0 + len(self.held)
            self.prod_tail = self.prod_pairs + cols * self.pairs
            self.prod_again = self.prod_tail + cols * self.tail
            self.sum_tail = self.sum0 + w * self.pairs + self.early
            self.sum_end = self.sum_tail + w * self.tail - self.early
            self.ends = (self.ring_again + self.again, self.prod_again + self.again, self.sum_end)
            self.after_row = self.again - min(BEFORE_ROW, self.again)

        def pair_sum(self, s, base):
            return self.sum0 + self.width * s + min(self.early, max(0, base - self.lag))

        def tail_sum(self, s):
            return self.sum_tail + (self.width - 1) * s + max(0, s - self.early)

    steps = []
    for t in range(-1, NP):
        steps.append(Step(t, steps[-1] if steps else None))
    final = steps[-1]

    def repeat(eng, count, unroll, body, first=0, apart=0):
        apart = min(apart, count)
        for s in range(first, first + apart):
            body(s, s, 0)
        first, count = first + apart, count - apart
        full = count // unroll
        if full >= 2:
            with eng.Fori(0, full) as i:
                for j in range(unroll):
                    body(i * unroll + (first + j), first + j, i)
        else:
            full = 0
        for s in range(first + full * unroll, first + count):
            body(s, s, 0)

    with ExitStack() as ctx:
        def sb(name, shape):
            return ctx.enter_context(nc.sbuf_tensor(name, shape, F32))

        def ps(name, shape):
            return ctx.enter_context(nc.psum_tensor(name, shape, F32))

        def sem(name):
            return ctx.enter_context(nc.semaphore(name))

        acc = sb("acc", [P, NP * W])
        part = sb("part", [P, NP * W])
        ring = sb("ring", [P, RING * K * W])
        held = sb("held", [P, (BAND + 1) * (BAND + 2) // 2 * K * W])
        block_sum = sb("block_sum", [P, SUMS * W])
        xin = sb("xin", [P, 2, W])
        y = sb("y", [P, 2, W])
        ones = sb("ones", [P, 1])
        neg_half = sb("neg_half", [P, K])
        ident = sb("ident", [P, P])
        lam_sb = sb("lam_sb", [P, 1])
        coef = sb("coef", [P, 8])
        alpha, beta = coef[:, 4:5], coef[:, 3:4]
        rs = sb("rs", [P, 5, K])
        d_all = sb("d_all", [P, NP * K])
        d_sq = sb("d_sq", [P, NP * K])
        own = sb("own", [P, NP * K])
        nbr = sb("nbr", [P, NP * K])
        stats = sb("stats", [P, 2, K, 6])
        mv = sb("mv", [P, 2, K, 2])
        rstd = sb("rstd", [P, 2, K])
        var_eps = sb("var_eps", [P, 2, K])
        shift = sb("shift", [P, 2, K])
        nmean = sb("nmean", [P, 2, K])

        prod = ps("prod", [P, BANKS * 512])
        row_ps = ps("row_ps", [P, 512])
        turned = ps("turned", [P, 2, 512])

        lane = [sem(f"ring_lane{j}") for j in range(LANES)]
        held_loaded = [sem(f"held_loaded{d}") for d in range(BAND + 1)]
        ring_free = sem("ring_free")
        summed = sem("summed")
        part_added = sem("part_added")
        multiplied = sem("multiplied")
        gathered = sem("gathered")
        row_summed = sem("row_summed")
        pow_asked = sem("pow_asked")
        pow_done = sem("pow_done")
        y_ready = sem("y_ready")
        x_loaded = [sem(f"x_loaded{j}") for j in range(2)]
        lam_loaded = sem("lam_loaded")
        pool_set = sem("pool_set")
        ident_set = sem("ident_set")
        dve_chain = sem("dve_chain")
        pool_chain = sem("pool_chain")
        scales_ready = sem("scales_ready")
        xe_loaded = [sem(f"xe_loaded{j}") for j in range(2)]
        transposed = sem("transposed")
        nbr_scaled = sem("nbr_scaled")
        own_scaled = sem("own_scaled")
        stats_done = sem("stats_done")
        norm_ready = sem("norm_ready")
        normed = sem("normed")
        stored = [sem(f"stored{j}") for j in range(2)]

        def slot(q):
            return ring[:, bass.ds((q % RING) * (K * W), K * W)]

        def held_slot(r, c):
            d = c - r
            s = d * (d + 1) // 2 + c % (d + 1)
            return held[:, s * K * W:(s + 1) * K * W]

        def adj_block(c, r):
            return adj_rows[bass.ds((c * NP + r) * P, P), :]

        def bank(m):
            return prod[:, bass.ds((m % BANKS) * 512, 512)]

        def sum_buf(e):
            return block_sum[:, bass.ds((e % SUMS) * W, W)]

        def panel(t, r):
            return t[:, bass.ds(r * W, W)]

        def wait_load(eng, base, per, unroll, i, extra=0):
            value = base // LANES + 1 + extra + i * (per * unroll // LANES)
            if not isinstance(value, int) or value > 0:
                eng.wait_ge(lane[base % LANES], value * 16)

        def wait_held(eng, r, c):
            eng.wait_ge(held_loaded[c - r], (r + 1) * 16)

        def pair_unroll(w):
            return LANES // w

        def epilogue_rows():
            return final.held + list(range(final.again))

        def result(e):
            return out_buf[:, (e % 2) * W:(e % 2 + 1) * W]

        out_buf = held[:, 0:2 * W]
        own_x = held[:, 2 * W:4 * W]
        mixed = held[:, 4 * W:(4 + MIXED) * W]

        block = ctx.enter_context(nc.Block())

        @block.sync
        def _(sp):
            sp.dma_start(lam_sb[:, :], lam[0:1, 0:1].to_broadcast([P, 1])).then_inc(lam_loaded, 16)

            def load(q, qbase, src, per, unroll, i):
                if qbase >= RING:
                    sp.wait_ge(ring_free, q - (RING - 1))
                wait_load(sp, qbase, per, unroll, i, extra=-1)
                sp.dma_start(slot(q), src).then_inc(lane[qbase % LANES], 16)

            for st in steps:
                t, w = st.t, st.width
                u = pair_unroll(w)

                def pair(s, base, i):
                    q, qb = st.ring0 + w * s, st.ring0 + w * base
                    load(q, qb, adj_block(LAST - s, t + 1), w, u, i)
                    if t >= 0:
                        load(q + 1, qb + 1, adj_block(t, s + (t + 1)), w, u, i)

                repeat(sp, st.pairs, u, pair, apart=RING if t < 0 else 0)
                if t >= 0:
                    for s in range(st.tail):
                        load(st.ring_tail + s, st.ring_tail + s, adj_block(t, t + 1 + st.pairs + s), 0, 0, 0)

                def again(s, base, i):
                    load(st.ring_again + s, st.ring_again + base, adj_block(t, s), 1, LANES, i)

                repeat(sp, st.again, LANES, again)

        @block.tensor
        def _(pe):
            def product(rhs, m, mbase, t):
                if mbase >= BANKS:
                    pe.wait_ge(gathered, m - (BANKS - 1))
                for k in range(K):
                    mm = pe.matmul(bank(m), y[:, t % 2, k * D:(k + 1) * D], rhs[:, k * W:(k + 1) * W],
                                   start=(k == 0), stop=(k == K - 1))
                mm.then_inc(multiplied, 1)

            def row_sums(r, sums):
                pe.wait_ge(part_added, sums)
                for k in range(K):
                    mm = pe.matmul(row_ps[:, k:k + 1], part[:, r * W + k:(r + 1) * W:K], ones[:, :],
                                   start=True, stop=True)
                mm.then_inc(row_summed, 1)

            def turn(e):
                r = epilogue_rows()[e]
                pe.wait_ge(gathered, final.prod0 + e + 1)
                if e == 0:
                    pe.wait_ge(ident_set, 1)
                if e >= 2:
                    pe.wait_ge(nbr_scaled, e - 1)
                for k in range(K):
                    mm = pe.transpose(turned[:, e % 2, k * P:(k + 1) * P],
                                      acc[:, r * W + k:(r + 1) * W:K], ident[:, :])
                mm.then_inc(transposed, 1)

            pe.wait_ge(pool_set, 1)
            for st in steps:
                t, w = st.t, st.width
                u = pair_unroll(w)
                if t >= 0:
                    pe.wait_ge(y_ready, t + 1)
                    def pair(s, base, i, m0=st.prod_pairs):
                        wait_load(pe, st.ring0 + w * base + 1, w, u, i)
                        product(slot(st.ring0 + 1 + w * s), m0 + s, m0 + base, t)

                    front = len(st.held) - st.between
                    for j, r in enumerate(st.held):
                        if j >= front:
                            pair(j - front, j - front, 0, m0=st.prod0 + j)
                        product(held_slot(r, t), st.held_prod[j], st.held_prod[j], t)
                    repeat(pe, st.pairs - st.between, u, pair, first=st.between,
                           apart=BANKS - 2 if t == 0 else 0)
                    for s in range(st.tail):
                        if st.row_early and s == ROW_AT:
                            row_sums(t + 1, st.sum_tail)
                        wait_load(pe, st.ring_tail + s, 0, 0, 0)
                        product(slot(st.ring_tail + s), st.prod_tail + s, st.prod_tail + s, t)

                if t == LAST:
                    break

                def again(s, base, i):
                    wait_load(pe, st.ring_again + base, 1, LANES, i)
                    product(slot(st.ring_again + s), st.prod_again + s, st.prod_again + base, t)

                repeat(pe, st.again - st.after_row, LANES, again)
                if not st.row_early:
                    row_sums(t + 1, st.sum_end)
                repeat(pe, st.after_row, LANES, again, first=st.again - st.after_row)

            for e in range(NP + TURN_LAG):
                if len(final.held) <= e < NP:
                    s = e - len(final.held)
                    wait_load(pe, final.ring_again + s, 0, 0, 0)
                    product(slot(final.ring_again + s), final.prod0 + e, final.prod0 + e, LAST)
                if e >= len(final.held):
                    for f in range(e - TURN_LAG if e > len(final.held) else 0, e - TURN_LAG + 1):
                        turn(f)

        @block.vector
        def _(dve):
            link_count = [0]

            def link(ins):
                link_count[0] += 1
                ins.then_inc(dve_chain, 1)
                dve.wait_ge(dve_chain, link_count[0])

            link(nc.vector.memset(ones[:, :], 1.0))
            dve.wait_ge(lam_loaded, 16)
            link(nc.vector.tensor_scalar(coef[:, 0:1], lam_sb[:, :], 0.0, 1.0, ALU.max, ALU.add))
            link(nc.vector.reciprocal(coef[:, 1:2], coef[:, 0:1]))
            link(nc.vector.tensor_scalar(coef[:, 2:3], coef[:, 0:1], 2.0, -2.0, ALU.mult, ALU.add))
            link(nc.vector.tensor_scalar(beta, coef[:, 1:2], 2.0, None, ALU.mult))
            link(nc.vector.tensor_tensor(alpha, coef[:, 2:3], coef[:, 1:2], ALU.mult))
            dve.wait_ge(pool_set, 1)

            def block_sums(src, e, ebase, done=None):
                if ebase >= SUMS:
                    dve.wait_ge(part_added, e - (SUMS - 1))
                nc.vector.tensor_reduce(sum_buf(e), src.rearrange("p (k i) -> p i k", k=K), AX.X,
                                        ALU.add).then_inc(summed, 1)

            def free_slots(sums, count):
                dve.wait_ge(summed, sums)
                dve.sem_inc(ring_free, count)

            def gather(m, r):
                nc.vector.tensor_tensor(panel(acc, r), panel(acc, r), bank(m), ALU.add).then_inc(gathered, 1)

            def scale_x(r):
                dve.wait_ge(row_summed, r + 1)
                link(nc.vector.tensor_scalar(rs[:, 0, :], row_ps[:, 0:K], beta, alpha, ALU.mult, ALU.add))
                link(nc.vector.tensor_scalar(rs[:, 1, :], rs[:, 0, :], 0.0, None, ALU.is_equal))
                nc.vector.tensor_tensor(rs[:, 2, :], rs[:, 0, :], rs[:, 1, :], ALU.add).then_inc(pow_asked, 1)
                link(nc.vector.tensor_scalar(rs[:, 3, :], rs[:, 1, :], -1.0, 1.0, ALU.mult, ALU.add))
                dve.wait_ge(pow_done, r + 1)
                d = d_all[:, r * K:(r + 1) * K]
                link(nc.vector.tensor_tensor(d, rs[:, 4, :], rs[:, 3, :], ALU.mult))
                dve.wait_ge(x_loaded[r % 2], 16 * (r // 2 + 1))
                nc.vector.tensor_tensor(y[:, r % 2, :].rearrange("p (k d) -> p k d", k=K),
                                        xin[:, r % 2, :].rearrange("p (k d) -> p k d", k=K),
                                        d.unsqueeze(2).to_broadcast([P, K, D]), ALU.mult).then_inc(y_ready, 1)

            for st in steps[:-1]:
                t, w = st.t, st.width
                u = pair_unroll(w)
                def pair(s, base, i, m0=st.prod_pairs):
                    q, e = st.ring0 + w * s, st.pair_sum(s, base)
                    qb, eb = st.ring0 + w * base, st.pair_sum(base, base)
                    wait_load(dve, qb, w, u, i)
                    block_sums(slot(q), e, eb)
                    if t >= 0:
                        wait_load(dve, qb + 1, w, u, i)
                        block_sums(slot(q + 1), e + 1, eb + 1)
                        dve.wait_ge(multiplied, m0 + s + 1)
                        free_slots(e + 2, 2)
                        gather(m0 + s, s + (t + 1))
                    else:
                        free_slots(e + 1, 1)
                    if 0 <= base - st.lag < st.early:
                        row_held(base - st.lag, e + w)

                def row_held(j, e):
                    c = LAST - st.pairs - j
                    wait_held(dve, t + 1, c)
                    block_sums(held_slot(t + 1, c), e, e)

                front = len(st.held) - st.between
                for j, r in enumerate(st.held):
                    if j >= front:
                        pair(j - front, j - front, 0, m0=st.prod0 + j)
                    dve.wait_ge(multiplied, st.held_prod[j] + 1)
                    gather(st.held_prod[j], r)
                repeat(dve, st.pairs - st.between, u, pair, first=st.between,
                       apart=max(0, st.lag + st.early - st.between))
                for s in range(st.tail):
                    q, e = st.ring_tail + s, st.tail_sum(s)
                    if s >= st.early:
                        row_held(s, e)
                        e += 1
                    if t >= 0:
                        wait_load(dve, q, 0, 0, 0)
                        block_sums(slot(q), e, e)
                        dve.wait_ge(multiplied, st.prod_tail + s + 1)
                        free_slots(e + 1, 1)
                        gather(st.prod_tail + s, t + 1 + st.pairs + s)
                    if st.row_early and s == ROW_AT:
                        scale_x(t + 1)

                def again(s, base, i):
                    dve.wait_ge(multiplied, st.prod_again + s + 1)
                    dve.sem_inc(ring_free, 1)
                    gather(st.prod_again + s, s)

                repeat(dve, st.again - st.after_row, LANES, again)
                if not st.row_early:
                    scale_x(t + 1)
                repeat(dve, st.after_row, LANES, again, first=st.again - st.after_row)

            dve.wait_ge(y_ready, NP)
            nc.vector.tensor_scalar(nbr[:, :], d_all[:, :], beta, None, ALU.mult)
            link(nc.vector.tensor_tensor(d_sq[:, :], d_all[:, :], d_all[:, :], ALU.mult))
            nc.vector.tensor_scalar(own[:, :], d_sq[:, :], alpha, 1.0, ALU.mult, ALU.add).then_inc(scales_ready, 1)

            def panel_stats(e):
                b = e % 2
                dve.wait_ge(nbr_scaled, e + 1)
                dve.wait_ge(own_scaled, e + 1)
                if e >= 2:
                    dve.wait_ge(norm_ready, e - 1)
                m = mixed[:, e % MIXED * W:(e % MIXED + 1) * W]
                link(nc.vector.tensor_tensor(m, m, own_x[:, b * W:(b + 1) * W], ALU.add))
                for k in range(K):
                    ins = nc.vector.bn_stats(stats[:, b, k, :], m[:, k * D:(k + 1) * D])
                link(ins)
                for k in range(K):
                    ins = nc.vector.bn_aggr(mv[:, b, k, :], stats[:, b, k, :])
                ins.then_inc(stats_done, 1)

            lag = TURN_LAG + 1
            for e in range(NP + lag):
                if e < NP:
                    dve.wait_ge(multiplied, final.prod0 + e + 1)
                    if e >= len(final.held):
                        dve.sem_inc(ring_free, 1)
                    gather(final.prod0 + e, epilogue_rows()[e])
                if e >= lag:
                    panel_stats(e - lag)

        @block.gpsimd
        def _(pool):
            link_count = [0]

            def link(ins):
                link_count[0] += 1
                ins.then_inc(pool_chain, 1)
                pool.wait_ge(pool_chain, link_count[0])

            nc.gpsimd.memset(part[:, :], 0.0)
            nc.gpsimd.memset(neg_half[:, :], -0.5)
            link(nc.gpsimd.memset(ident[:, :], 0.0))
            nc.gpsimd.affine_select(out=ident[:, :], in_=ident[:, :], compare_op=ALU.not_equal, fill=1.0,
                                    base=0, pattern=[[-1, P]], channel_multiplier=1).then_inc(ident_set, 1)
            nc.gpsimd.memset(acc[:, :], 0.0).then_inc(pool_set, 1)
            pool.wait_ge(pool_set, 1)

            def add_sums(e, ebase, r):
                pool.wait_ge(summed, e + 1)
                if ebase >= 1:
                    pool.wait_ge(part_added, e)
                nc.gpsimd.tensor_tensor(panel(part, r), panel(part, r), sum_buf(e),
                                        ALU.add).then_inc(part_added, 1)

            for st in steps[:-1]:
                t, w = st.t, st.width

                def pair(s, base, i):
                    e, eb = st.pair_sum(s, base), st.pair_sum(base, base)
                    add_sums(e, eb, t + 1)
                    if t >= 0:
                        add_sums(e + 1, eb + 1, s + (t + 1))
                    if 0 <= base - st.lag < st.early:
                        add_sums(e + w, eb + w, t + 1)

                def power():
                    pool.wait_ge(pow_asked, t + 2)
                    nc.gpsimd.tensor_tensor(rs[:, 4, :], rs[:, 2, :], neg_half[:, :],
                                            ALU.pow).then_inc(pow_done, 1)

                repeat(pool, st.pairs, 2, pair, apart=min(st.pairs, st.lag + st.early))
                for s in range(st.tail):
                    e = st.tail_sum(s)
                    if s >= st.early:
                        add_sums(e, e, t + 1)
                        e += 1
                    if t >= 0:
                        add_sums(e, e, t + 1 + st.pairs + s)
                    if st.row_early and s == ROW_AT:
                        power()
                if not st.row_early:
                    power()

            def norm_scales(e):
                b = e % 2
                pool.wait_ge(stats_done, e + 1)
                if e >= 2:
                    pool.wait_ge(normed, e - 1)
                nc.gpsimd.tensor_scalar(nmean[:, b, :], mv[:, b, :, 0], -1.0, None, ALU.mult)
                link(nc.gpsimd.tensor_scalar(var_eps[:, b, :], mv[:, b, :, 1], EPS, None, ALU.add))
                link(nc.gpsimd.tensor_tensor(rstd[:, b, :], var_eps[:, b, :], neg_half[:, :], ALU.pow))
                nc.gpsimd.tensor_tensor(shift[:, b, :], nmean[:, b, :], rstd[:, b, :],
                                        ALU.mult).then_inc(norm_ready, 1)

            pool.wait_ge(scales_ready, 1)
            pool.wait_ge(multiplied, final.prod_pairs)
            for e in range(NP + 1):
                if e < NP:
                    r, b = epilogue_rows()[e], e % 2
                    pool.wait_ge(xe_loaded[b], 16 * (e // 2 + 1))
                    if e >= 2:
                        pool.wait_ge(stats_done, e - 1)
                    nc.gpsimd.tensor_tensor(
                        own_x[:, b * W:(b + 1) * W].rearrange("p (k d) -> p k d", k=K),
                        xin[:, b, :].rearrange("p (k d) -> p k d", k=K),
                        own[:, r * K:(r + 1) * K].unsqueeze(2).to_broadcast([P, K, D]),
                        ALU.mult).then_inc(own_scaled, 1)
                if e >= 1:
                    norm_scales(e - 1)

        @block.scalar
        def _(act):
            for st in steps[:-1]:
                t, r = st.t, st.t + 1
                for s in range(st.tail):
                    c = LAST - st.pairs - s
                    d = c - r
                    if t >= d:
                        act.wait_ge(multiplied, st.held_prod[st.held.index(t - d)] + 1)
                    if r >= 1:
                        wait_held(act, r - 1, r - 1 + d)
                    act.dma_start(held_slot(r, c), adj_block(c, r)).then_inc(held_loaded[d], 16)
                if r >= 2:
                    act.wait_ge(y_ready, r - 1)
                act.dma_start(xin[:, r % 2, :], x_rows[r * P:(r + 1) * P, :]).then_inc(x_loaded[r % 2], 16)

            def load_x(e):
                r = epilogue_rows()[e]
                if e >= 2:
                    act.wait_ge(own_scaled, e - 1)
                act.dma_start(xin[:, e % 2, :], x_rows[r * P:(r + 1) * P, :]).then_inc(xe_loaded[e % 2], 16)

            act.wait_ge(scales_ready, 1)
            load_x(0)
            act.wait_ge(multiplied, final.prod_pairs)
            for e in range(NP + 2):
                if e + 1 < NP:
                    load_x(e + 1)
                if e < NP:
                    r, b = epilogue_rows()[e], e % 2
                    act.wait_ge(transposed, e + 1)
                    m0 = e % MIXED * W
                    if e >= MIXED:
                        act.wait_ge(stats_done, e - MIXED + 1)
                    for k in range(K):
                        ins = nc.scalar.activation(mixed[:, m0 + k * D:m0 + (k + 1) * D],
                                                   turned[:, b, k * P:(k + 1) * P], ACT.Copy,
                                                   scale=nbr[:, r * K + k:r * K + k + 1])
                    ins.then_inc(nbr_scaled, 1)
                if e >= 2:
                    f, b = e - 2, e % 2
                    m0 = f % MIXED * W
                    act.wait_ge(norm_ready, f + 1)
                    if f >= 2:
                        act.wait_ge(stored[b], 16 * (f // 2))
                    for k in range(K):
                        ins = nc.scalar.activation(result(f)[:, k * D:(k + 1) * D],
                                                   mixed[:, m0 + k * D:m0 + (k + 1) * D], ACT.Identity,
                                                   bias=shift[:, b, k:k + 1], scale=rstd[:, b, k:k + 1])
                    ins.then_inc(normed, 1)
                    r = epilogue_rows()[f]
                    act.wait_ge(normed, f + 1)
                    act.dma_start(out_rows[r * P:(r + 1) * P, :], result(f)).then_inc(stored[b], 16)
            for j in range(2):
                act.wait_ge(stored[j], 16 * (NP // 2))


def kernel(x, adj, L0_gnn_lambda_):
    import numpy as np
    import concourse.bacc as bacc
    from concourse.bass_utils import run_bass_kernel_spmd

    x, adj, lam = np.asarray(x), np.asarray(adj), np.asarray(L0_gnn_lambda_)
    NP = x.shape[0] // W
    blocks = adj.reshape(NP, W, NP, P, K).transpose(2, 0, 3, 4, 1).reshape(NP, NP, P, K * W)
    arrays = {"x_dram": np.ascontiguousarray(x), "adj_dram": np.ascontiguousarray(blocks),
              "lam_dram": np.ascontiguousarray(lam.reshape(1, 1))}
    nc = bacc.Bacc("TRN2", target_bir_lowering=False, num_devices=1)
    args = [nc.dram_tensor(n, a.shape, mybir.dt.from_np(a.dtype), kind="ExternalInput").ap()
            for n, a in arrays.items()]
    out = nc.dram_tensor("out_dram", x.shape, F32, kind="ExternalOutput").ap()
    gnn_resnorm(nc, *args, out)
    r = run_bass_kernel_spmd(nc, [arrays], core_ids=[0])
    return r.results[0]["out_dram"]
```

```python
from contextlib import ExitStack

import concourse.bass as bass
from concourse import mybir

ALU = mybir.AluOpType
ACT = mybir.ActivationFunctionType
AX = mybir.AxisListType
F32 = mybir.dt.float32
F32R = mybir.dt.float32r

P = 128
K = 4
W = P * K
D = 128
EPS = 1e-5

BAND = 3
RING = 6
LANES = 4
BANKS = 4
TURN_LAG = 2
HELD_LAG = 2
ROW_AT = 2
BEFORE_ROW = 3
HELD_AFTER = 2
HI_BUFS = 6
LO_BUFS = 2
XGROUP = BAND + 1
OWN_LEAD = 3
OUTS = 4
MIXED = 4
BY_DVE = 2
SPLIT_ROW_AT = 1
SUMS = 2


def gnn_resnorm(nc, x, adj, lam, out):
    N = x.shape[0]
    NP = N // W
    LAST = NP - 1

    adj_rows = adj.rearrange("c r p f -> (c r p) f")
    x_rows = x.rearrange("(r p k) d -> (r p) (k d)", p=P, k=K)
    out_rows = out.rearrange("(r p k) d -> (r p) (k d)", p=P, k=K)

    class Step:
        def __init__(self, t, before):
            self.t = t
            self.held = [r for r in range(t - BAND, t + 1) if r >= 0] if t >= 0 else []
            self.pairs = max(0, LAST - (t + 1 + BAND))
            self.tail = LAST - t - self.pairs
            self.again = max(0, t - BAND)
            self.width = 2 if t >= 0 else 1
            if before is None:
                self.ring0 = self.prod0 = self.sum0 = 0
            else:
                self.ring0, self.prod0, self.sum0 = before.ends
            w, cols = self.width, self.width - 1
            self.between = min(self.pairs, len(self.held))
            front = len(self.held) - self.between
            self.held_prod = [self.prod0 + j + max(0, j - front + 1) for j in range(len(self.held))]
            self.ring_tail = self.ring0 + w * self.pairs
            self.ring_again = self.ring_tail + cols * self.tail
            self.lag = HELD_LAG if t >= 0 else 1
            self.early = min(self.tail, max(0, self.pairs - self.lag))
            self.row_early = t >= 0 and self.early == self.tail
            self.prod_pairs = self.prod0 + len(self.held)
            self.prod_tail = self.prod_pairs + cols * self.pairs
            self.prod_again = self.prod_tail + cols * self.tail
            self.sum_tail = self.sum0 + w * self.pairs + self.early
            self.sum_end = self.sum_tail + w * self.tail - self.early
            self.ends = (self.ring_again + self.again, self.prod_again + self.again, self.sum_end)
            self.row_after = self.tail + SPLIT_ROW_AT
            self.after_row = self.again - min(BEFORE_ROW, self.again)

        def pair_sum(self, s, base):
            return self.sum0 + self.width * s + min(self.early, max(0, base - self.lag))

        def tail_sum(self, s):
            return self.sum_tail + (self.width - 1) * s + max(0, s - self.early)

    steps = []
    for t in range(-1, NP):
        steps.append(Step(t, steps[-1] if steps else None))
    final = steps[-1]

    def repeat(eng, count, unroll, body, first=0, apart=0):
        apart = min(apart, count)
        for s in range(first, first + apart):
            body(s, s, 0)
        first, count = first + apart, count - apart
        full = count // unroll
        if full >= 2:
            with eng.Fori(0, full) as i:
                for j in range(unroll):
                    body(i * unroll + (first + j), first + j, i)
        else:
            full = 0
        for s in range(first + full * unroll, first + count):
            body(s, s, 0)

    with ExitStack() as ctx:
        def sb(name, shape):
            return ctx.enter_context(nc.sbuf_tensor(name, shape, F32))

        def ps(name, shape):
            return ctx.enter_context(nc.psum_tensor(name, shape, F32))

        def sem(name):
            return ctx.enter_context(nc.semaphore(name))

        acc = sb("acc", [P, NP * W])
        block_sum = sb("block_sum", [P, SUMS * W])
        xin = sb("xin", [P, 2, W])
        y = sb("y", [P, 2, W])
        ones = sb("ones", [P, 1])
        neg_half = sb("neg_half", [P, K])
        ident = sb("ident", [P, P])
        lam_sb = sb("lam_sb", [P, 1])
        coef = sb("coef", [P, 8])
        alpha, beta = coef[:, 4:5], coef[:, 3:4]
        rs = sb("rs", [P, 5, K])
        d_all = sb("d_all", [P, NP * K])
        d_sq = sb("d_sq", [P, NP * K])
        own = sb("own", [P, NP * K])
        nbr = sb("nbr", [P, NP * K])
        stats = sb("stats", [P, 2, K, 6])
        mv = sb("mv", [P, 2, K, 2])
        rstd = sb("rstd", [P, 2, K])
        var_eps = sb("var_eps", [P, 2, K])
        shift = sb("shift", [P, 2, K])
        nmean = sb("nmean", [P, 2, K])

        ring_shape = [P, RING * K * W]
        held_shape = [P, (BAND + 1) * (BAND + 2) // 2 * K * W]
        with ExitStack() as early:
            ring = early.enter_context(nc.sbuf_tensor("ring", ring_shape, F32))
            held = early.enter_context(nc.sbuf_tensor("held", held_shape, F32))
            part = early.enter_context(nc.sbuf_tensor("part", [P, NP * W], F32))

        def sb_r(name, shape):
            return ctx.enter_context(nc.sbuf_tensor(name, shape, F32R))

        ring_r = sb_r("ring_r", ring_shape)
        held_r = sb_r("held_r", held_shape)
        hi = sb_r("hi", [P, HI_BUFS, W])
        lo = sb_r("lo", [P, LO_BUFS, W])
        y_hi = sb_r("y_hi", [P, 2, W])
        y_lo = sb_r("y_lo", [P, 2, W])
        first_split = HI_BUFS + LO_BUFS + 4 - 1

        prod = ps("prod", [P, BANKS * 512])
        row_ps = ps("row_ps", [P, 512])
        turned = ps("turned", [P, 2, 512])

        lane = [sem(f"ring_lane{j}") for j in range(LANES)]
        held_loaded = [sem(f"held_loaded{d}") for d in range(BAND + 1)]
        ring_free = sem("ring_free")
        hi_ready = sem("hi_ready")
        lo_by_dve = sem("lo_by_dve")
        lo_by_pool = sem("lo_by_pool")
        slices_used = sem("slices_used")
        summed = sem("summed")
        part_added = sem("part_added")
        multiplied = sem("multiplied")
        gathered = sem("gathered")
        row_summed = sem("row_summed")
        pow_asked = sem("pow_asked")
        pow_done = sem("pow_done")
        y_ready = sem("y_ready")
        x_loaded = [sem(f"x_loaded{j}") for j in range(2)]
        lam_loaded = sem("lam_loaded")
        pool_set = sem("pool_set")
        ident_set = sem("ident_set")
        dve_chain = sem("dve_chain")
        pool_chain = sem("pool_chain")
        scales_ready = sem("scales_ready")
        xe_loaded = [sem(f"xe_loaded{j}") for j in range(NP // XGROUP)]
        transposed = sem("transposed")
        nbr_scaled = sem("nbr_scaled")
        own_scaled = sem("own_scaled")
        stats_done = sem("stats_done")
        norm_ready = sem("norm_ready")
        normed_by_act = sem("normed_by_act")
        normed_by_dve = sem("normed_by_dve")
        stored = [sem(f"stored{j}") for j in range(OUTS)]

        def slot(q, ring=ring):
            return ring[:, bass.ds((q % RING) * (K * W), K * W)]

        def held_slot(r, c, held=held):
            d = c - r
            s = d * (d + 1) // 2 + c % (d + 1)
            return held[:, s * K * W:(s + 1) * K * W]

        def adj_block(c, r):
            return adj_rows[bass.ds((c * NP + r) * P, P), :]

        def bank(m):
            return prod[:, bass.ds((m % BANKS) * 512, 512)]

        def sum_buf(e):
            return block_sum[:, bass.ds((e % SUMS) * W, W)]

        def panel(t, r):
            return t[:, bass.ds(r * W, W)]

        def wait_load(eng, base, per, unroll, i, extra=0):
            value = base // LANES + 1 + extra + i * (per * unroll // LANES)
            if not isinstance(value, int) or value > 0:
                eng.wait_ge(lane[base % LANES], value * 16)

        def wait_held(eng, r, c):
            eng.wait_ge(held_loaded[c - r], (r + 1) * 16)

        def is_split(st):
            return first_split <= st.t

        class Item:

            def __init__(self, st, j, kind, s, q):
                self.st, self.j, self.m, self.q = st, j, st.prod0 + j, q
                self.held, self.tail, self.again = [s if kind == k else None for k in ("held", "tail", "again")]
                if kind == "held":
                    self.row = st.held[s]
                    self.src, self.src_r = held_slot(self.row, st.t), held_slot(self.row, st.t, held_r)
                else:
                    self.row = st.t + 1 + s if kind == "tail" else s
                    self.src, self.src_r = slot(q), slot(q, ring_r)
                self.sum = st.tail_sum(s) if kind == "tail" else None
                self.held_sum = st.tail_sum(s) + 1 if kind == "again" and s < st.tail else None
                light = self.sum is None and self.held_sum is None
                if st is final and kind == "again":
                    self.cut = [(0, "dve")]
                elif light:
                    self.cut = [(0, "dve"), (1, "pool"), (2, "dve"), (3, "pool")]
                else:
                    self.cut = [(0, "dve"), (1, "pool")]
                assert self.tail is None or len(self.cut) <= LO_BUFS
                self.lo_before = max((x.m for x in split_items if x.tail is not None), default=None)
                self.numbers = []
                for k, by in self.cut:
                    n = len(slices)
                    slices.append((by, k, self.m))
                    self.numbers.append((n, k, by, [s[0] for s in slices].count(by)))

            def lo(self, k):
                if self.tail is None:
                    return self.src_r[:, k * W:(k + 1) * W]
                return lo[:, k, :]

            def wait_lo(self, eng):
                if self.tail is not None and self.lo_before is not None:
                    eng.wait_ge(multiplied, self.lo_before + 1)

            def wait(self, eng):
                if self.held is None:
                    wait_load(eng, self.q, 0, 0, 0)
                else:
                    wait_held(eng, self.row, self.st.t)

        def wait_slice_used(eng, n):
            _, k, m = slices[n]
            if k == K - 1:
                eng.wait_ge(multiplied, m + 1)
            else:
                eng.wait_ge(slices_used, sum(s[1] < K - 1 for s in slices[:n + 1]))

        slices = []
        split_items = []
        for st in steps:
            if is_split(st):
                assert st.pairs == 0 and st.again > st.tail
                order = [("held", s) for s in range(len(st.held))]
                for s in range(st.again):
                    if s < st.tail:
                        order.append(("tail", s))
                    order.append(("again", s))
                q = st.ring_tail
                for j, (kind, s) in enumerate(order):
                    split_items.append(Item(st, j, kind, s, q))
                    q += kind != "held"

        def step_items(st):
            return [x for x in split_items if x.st is st]

        def next_item(x):
            n = x.m - split_items[0].m + 1
            return split_items[n] if n < len(split_items) else None

        def pair_unroll(w):
            return LANES // w

        def epilogue_rows():
            return final.held + list(range(final.again))

        def result(e):
            return out_buf[:, e % OUTS * W:(e % OUTS + 1) * W]

        def wait_normed(eng, f):
            if f < NP - BY_DVE:
                eng.wait_ge(normed_by_act, f + 1)
            else:
                eng.wait_ge(normed_by_dve, f - (NP - BY_DVE) + 1)

        out_buf = held_slot(LAST, LAST)
        mixed = held_slot(LAST - 2, LAST - 1)
        x_groups = [held_slot(c - d, c) for c in (LAST - 2, LAST - 1) for d in (BAND - 1, BAND)]

        def own_x(e):
            return x_groups[e // XGROUP][:, e % XGROUP * W:(e % XGROUP + 1) * W]

        block = ctx.enter_context(nc.Block())

        @block.sync
        def _(sp):
            sp.dma_start(lam_sb[:, :], lam[0:1, 0:1].to_broadcast([P, 1])).then_inc(lam_loaded, 16)

            def load(q, qbase, src, per, unroll, i):
                if qbase >= RING:
                    sp.wait_ge(ring_free, q - (RING - 1))
                wait_load(sp, qbase, per, unroll, i, extra=-1)
                sp.dma_start(slot(q), src).then_inc(lane[qbase % LANES], 16)

            for st in steps:
                t, w = st.t, st.width
                u = pair_unroll(w)
                if is_split(st):
                    for x in step_items(st):
                        if x.held is None:
                            load(x.q, x.q, adj_block(t, x.row), 0, 0, 0)
                    continue

                def pair(s, base, i):
                    q, qb = st.ring0 + w * s, st.ring0 + w * base
                    load(q, qb, adj_block(LAST - s, t + 1), w, u, i)
                    if t >= 0:
                        load(q + 1, qb + 1, adj_block(t, s + (t + 1)), w, u, i)

                repeat(sp, st.pairs, u, pair, apart=RING if t < 0 else 0)
                if t >= 0:
                    for s in range(st.tail):
                        load(st.ring_tail + s, st.ring_tail + s, adj_block(t, t + 1 + st.pairs + s), 0, 0, 0)

                def again(s, base, i):
                    load(st.ring_again + s, st.ring_again + base, adj_block(t, s), 1, LANES, i)

                repeat(sp, st.again, LANES, again)

            for f in range(NP - BY_DVE, NP):
                r = epilogue_rows()[f]
                wait_normed(sp, f)
                sp.dma_start(out_rows[r * P:(r + 1) * P, :], result(f)).then_inc(stored[f % OUTS], 16)
            for j in range(OUTS):
                sp.wait_ge(stored[j], NP // OUTS * 16)

        @block.tensor
        def _(pe):
            def product(rhs, m, mbase, t):
                if mbase >= BANKS:
                    pe.wait_ge(gathered, m - (BANKS - 1))
                for k in range(K):
                    mm = pe.matmul(bank(m), y[:, t % 2, k * D:(k + 1) * D], rhs[:, k * W:(k + 1) * W],
                                   start=(k == 0), stop=(k == K - 1))
                mm.then_inc(multiplied, 1)

            def row_sums(r, sums):
                pe.wait_ge(part_added, sums)
                for k in range(K):
                    mm = pe.matmul(row_ps[:, k:k + 1], part[:, r * W + k:(r + 1) * W:K], ones[:, :],
                                   start=True, stop=True)
                mm.then_inc(row_summed, 1)

            def turn(e):
                r = epilogue_rows()[e]
                pe.wait_ge(gathered, final.prod0 + e + 1)
                if e == 0:
                    pe.wait_ge(ident_set, 1)
                if e >= 2:
                    pe.wait_ge(nbr_scaled, e - 1)
                for k in range(K):
                    mm = pe.transpose(turned[:, e % 2, k * P:(k + 1) * P],
                                      acc[:, r * W + k:(r + 1) * W:K], ident[:, :])
                mm.then_inc(transposed, 1)

            def split_product(x):
                p, t = x.st.t % 2, x.st.t
                pe.wait_ge(gathered, x.m - (BANKS - 1))
                for n, k, by, count in x.numbers:
                    b = n % HI_BUFS
                    pe.wait_ge(lo_by_dve if by == "dve" else lo_by_pool, count)
                    cols = slice(k * D, (k + 1) * D)
                    pe.matmul(bank(x.m), y_hi[:, p, cols], hi[:, b, :], start=(k == 0), stop=False)
                    pe.matmul(bank(x.m), y_hi[:, p, cols], x.lo(k), start=False, stop=False)
                    mm = pe.matmul(bank(x.m), y_lo[:, p, cols], hi[:, b, :], start=False, stop=(k == K - 1))
                    if k < K - 1:
                        mm.then_inc(slices_used, 1)
                for k in range(len(x.cut), K):
                    mm = pe.matmul(bank(x.m), y[:, p, k * D:(k + 1) * D], x.src[:, k * W:(k + 1) * W],
                                   start=False, stop=(k == K - 1))
                mm.then_inc(multiplied, 1)

            pe.wait_ge(pool_set, 1)
            for st in steps:
                t, w = st.t, st.width
                u = pair_unroll(w)
                if is_split(st):
                    pe.wait_ge(y_ready, t + 1)
                    for x in step_items(st):
                        x.wait(pe)
                        split_product(x)
                        if st is final and x.j >= TURN_LAG:
                            turn(x.j - TURN_LAG)
                        elif x.again == st.row_after:
                            row_sums(t + 1, st.sum_end)
                    continue
                if t >= 0:
                    pe.wait_ge(y_ready, t + 1)
                    def pair(s, base, i, m0=st.prod_pairs):
                        wait_load(pe, st.ring0 + w * base + 1, w, u, i)
                        product(slot(st.ring0 + 1 + w * s), m0 + s, m0 + base, t)

                    front = len(st.held) - st.between
                    for j, r in enumerate(st.held):
                        if j >= front:
                            pair(j - front, j - front, 0, m0=st.prod0 + j)
                        product(held_slot(r, t), st.held_prod[j], st.held_prod[j], t)
                    repeat(pe, st.pairs - st.between, u, pair, first=st.between,
                           apart=BANKS - 2 if t == 0 else 0)
                    for s in range(st.tail):
                        if st.row_early and s == ROW_AT:
                            row_sums(t + 1, st.sum_tail)
                        wait_load(pe, st.ring_tail + s, 0, 0, 0)
                        product(slot(st.ring_tail + s), st.prod_tail + s, st.prod_tail + s, t)

                def again(s, base, i):
                    wait_load(pe, st.ring_again + base, 1, LANES, i)
                    product(slot(st.ring_again + s), st.prod_again + s, st.prod_again + base, t)

                repeat(pe, st.again - st.after_row, LANES, again)
                if not st.row_early:
                    row_sums(t + 1, st.sum_end)
                repeat(pe, st.after_row, LANES, again, first=st.again - st.after_row)

            for e in range(NP - TURN_LAG, NP):
                turn(e)

        @block.vector
        def _(dve):
            link_count = [0]

            def link(ins):
                link_count[0] += 1
                ins.then_inc(dve_chain, 1)
                dve.wait_ge(dve_chain, link_count[0])

            link(nc.vector.memset(ones[:, :], 1.0))
            dve.wait_ge(lam_loaded, 16)
            link(nc.vector.tensor_scalar(coef[:, 0:1], lam_sb[:, :], 0.0, 1.0, ALU.max, ALU.add))
            link(nc.vector.reciprocal(coef[:, 1:2], coef[:, 0:1]))
            link(nc.vector.tensor_scalar(coef[:, 2:3], coef[:, 0:1], 2.0, -2.0, ALU.mult, ALU.add))
            link(nc.vector.tensor_scalar(beta, coef[:, 1:2], 2.0, None, ALU.mult))
            link(nc.vector.tensor_tensor(alpha, coef[:, 2:3], coef[:, 1:2], ALU.mult))
            dve.wait_ge(pool_set, 1)

            def block_sums(src, e, ebase):
                if ebase >= SUMS:
                    dve.wait_ge(part_added, e - (SUMS - 1))
                nc.vector.tensor_reduce(sum_buf(e), src.rearrange("p (k i) -> p i k", k=K), AX.X,
                                        ALU.add).then_inc(summed, 1)

            def free_slots(sums, count):
                dve.wait_ge(summed, sums)
                dve.sem_inc(ring_free, count)

            def gather(m, r):
                nc.vector.tensor_tensor(panel(acc, r), panel(acc, r), bank(m), ALU.add).then_inc(gathered, 1)

            def scale_x(r, beside=None):
                dve.wait_ge(row_summed, r + 1)
                link(nc.vector.tensor_scalar(rs[:, 0, :], row_ps[:, 0:K], beta, alpha, ALU.mult, ALU.add))
                link(nc.vector.tensor_scalar(rs[:, 1, :], rs[:, 0, :], 0.0, None, ALU.is_equal))
                nc.vector.tensor_tensor(rs[:, 2, :], rs[:, 0, :], rs[:, 1, :], ALU.add).then_inc(pow_asked, 1)
                link(nc.vector.tensor_scalar(rs[:, 3, :], rs[:, 1, :], -1.0, 1.0, ALU.mult, ALU.add))
                if beside:
                    split_lo(beside, beside.numbers[:1])
                dve.wait_ge(pow_done, r + 1)
                d = d_all[:, r * K:(r + 1) * K]
                link(nc.vector.tensor_tensor(d, rs[:, 4, :], rs[:, 3, :], ALU.mult))
                dve.wait_ge(x_loaded[r % 2], 16 * (r // 2 + 1))
                ins = nc.vector.tensor_tensor(y[:, r % 2, :].rearrange("p (k d) -> p k d", k=K),
                                              xin[:, r % 2, :].rearrange("p (k d) -> p k d", k=K),
                                              d.unsqueeze(2).to_broadcast([P, K, D]), ALU.mult)
                if first_split <= r:
                    link(ins)
                    if beside:
                        split_lo(beside, beside.numbers[1:])
                    link(nc.vector.tensor_copy(y_hi[:, r % 2, :], y[:, r % 2, :]))
                    ins = nc.vector.tensor_tensor(y_lo[:, r % 2, :], y[:, r % 2, :],
                                                  y_hi[:, r % 2, :].bitcast(F32), ALU.subtract)
                ins.then_inc(y_ready, 1)

            def split_lo(x, numbers=None):
                for n, k, by, _ in numbers or x.numbers:
                    if by != "dve":
                        continue
                    dve.wait_ge(hi_ready, n + 1)
                    x.wait_lo(dve)
                    nc.vector.tensor_tensor(x.lo(k), x.src[:, k * W:(k + 1) * W],
                                            hi[:, n % HI_BUFS, :].bitcast(F32), ALU.subtract).then_inc(lo_by_dve, 1)

            for st in steps[:-1]:
                t, w = st.t, st.width
                u = pair_unroll(w)
                if is_split(st):
                    for x in step_items(st):
                        if x is split_items[0]:
                            split_lo(x)
                        if next_item(x) and x.again != st.row_after + 1:
                            split_lo(next_item(x))
                        if x.sum is not None:
                            wait_load(dve, x.q, 0, 0, 0)
                            block_sums(x.src, x.sum, x.sum)
                        if x.held_sum is not None:
                            c = LAST - x.again
                            wait_held(dve, t + 1, c)
                            block_sums(held_slot(t + 1, c), x.held_sum, x.held_sum)
                        dve.wait_ge(multiplied, x.m + 1)
                        if x.sum is not None:
                            free_slots(x.sum + 1, 1)
                        if x.again is not None:
                            dve.sem_inc(ring_free, 1)
                        gather(x.m, x.row)
                        if x.again == st.row_after:
                            scale_x(t + 1, beside=next_item(next_item(x)))
                    continue
                def pair(s, base, i, m0=st.prod_pairs):
                    q, e = st.ring0 + w * s, st.pair_sum(s, base)
                    qb, eb = st.ring0 + w * base, st.pair_sum(base, base)
                    wait_load(dve, qb, w, u, i)
                    block_sums(slot(q), e, eb)
                    if t >= 0:
                        wait_load(dve, qb + 1, w, u, i)
                        block_sums(slot(q + 1), e + 1, eb + 1)
                        dve.wait_ge(multiplied, m0 + s + 1)
                        free_slots(e + 2, 2)
                        gather(m0 + s, s + (t + 1))
                    else:
                        free_slots(e + 1, 1)
                    if 0 <= base - st.lag < st.early:
                        row_held(base - st.lag, e + w)

                def row_held(j, e):
                    c = LAST - st.pairs - j
                    wait_held(dve, t + 1, c)
                    block_sums(held_slot(t + 1, c), e, e)

                front = len(st.held) - st.between
                for j, r in enumerate(st.held):
                    if j >= front:
                        pair(j - front, j - front, 0, m0=st.prod0 + j)
                    dve.wait_ge(multiplied, st.held_prod[j] + 1)
                    gather(st.held_prod[j], r)
                repeat(dve, st.pairs - st.between, u, pair, first=st.between,
                       apart=max(0, st.lag + st.early - st.between))
                for s in range(st.tail):
                    q, e = st.ring_tail + s, st.tail_sum(s)
                    if s >= st.early:
                        row_held(s, e)
                        e += 1
                    if t >= 0:
                        wait_load(dve, q, 0, 0, 0)
                        block_sums(slot(q), e, e)
                        dve.wait_ge(multiplied, st.prod_tail + s + 1)
                        free_slots(e + 1, 1)
                        gather(st.prod_tail + s, t + 1 + st.pairs + s)
                    if st.row_early and s == ROW_AT:
                        scale_x(t + 1)

                def again(s, base, i):
                    dve.wait_ge(multiplied, st.prod_again + s + 1)
                    dve.sem_inc(ring_free, 1)
                    gather(st.prod_again + s, s)

                repeat(dve, st.again - st.after_row, LANES, again)
                if not st.row_early:
                    scale_x(t + 1)
                repeat(dve, st.after_row, LANES, again, first=st.again - st.after_row)

            dve.wait_ge(y_ready, NP)
            nc.vector.tensor_scalar(nbr[:, :], d_all[:, :], beta, None, ALU.mult)
            link(nc.vector.tensor_tensor(d_sq[:, :], d_all[:, :], d_all[:, :], ALU.mult))
            nc.vector.tensor_scalar(own[:, :], d_sq[:, :], alpha, 1.0, ALU.mult, ALU.add).then_inc(scales_ready, 1)

            def panel_stats(e):
                b = e % 2
                dve.wait_ge(nbr_scaled, e + 1)
                dve.wait_ge(own_scaled, e + 1)
                if e >= 2:
                    dve.wait_ge(norm_ready, e - 1)
                m = mixed[:, e % MIXED * W:(e % MIXED + 1) * W]
                link(nc.vector.tensor_tensor(m, m, own_x(e), ALU.add))
                for k in range(K):
                    ins = nc.vector.bn_stats(stats[:, b, k, :], m[:, k * D:(k + 1) * D])
                link(ins)
                for k in range(K):
                    ins = nc.vector.bn_aggr(mv[:, b, k, :], stats[:, b, k, :])
                ins.then_inc(stats_done, 1)

            def normalise(f):
                m0, b, o = f % MIXED * W, f % 2, f % OUTS
                dve.wait_ge(norm_ready, f + 1)
                dve.wait_ge(stored[o], f // OUTS * 16)
                for k in range(K):
                    ins = nc.vector.tensor_scalar(result(f)[:, k * D:(k + 1) * D],
                                                  mixed[:, m0 + k * D:m0 + (k + 1) * D],
                                                  rstd[:, b, k:k + 1], shift[:, b, k:k + 1], ALU.mult, ALU.add)
                ins.then_inc(normed_by_dve, 1)

            lag, items = TURN_LAG + 1, step_items(final)
            for e in range(NP + lag):
                if e < NP:
                    if e + 1 < NP:
                        split_lo(items[e + 1])
                    dve.wait_ge(multiplied, final.prod0 + e + 1)
                    if e >= len(final.held):
                        dve.sem_inc(ring_free, 1)
                    gather(final.prod0 + e, items[e].row)
                if e >= lag:
                    panel_stats(e - lag)
            for f in range(NP - BY_DVE, NP):
                normalise(f)

        @block.gpsimd
        def _(pool):
            link_count = [0]

            def link(ins):
                link_count[0] += 1
                ins.then_inc(pool_chain, 1)
                pool.wait_ge(pool_chain, link_count[0])

            nc.gpsimd.memset(part[:, :], 0.0)
            nc.gpsimd.memset(neg_half[:, :], -0.5)
            link(nc.gpsimd.memset(ident[:, :], 0.0))
            nc.gpsimd.affine_select(out=ident[:, :], in_=ident[:, :], compare_op=ALU.not_equal, fill=1.0,
                                    base=0, pattern=[[-1, P]], channel_multiplier=1).then_inc(ident_set, 1)
            nc.gpsimd.memset(acc[:, :], 0.0).then_inc(pool_set, 1)
            pool.wait_ge(pool_set, 1)

            def add_sums(e, ebase, r):
                pool.wait_ge(summed, e + 1)
                if ebase >= 1:
                    pool.wait_ge(part_added, e)
                nc.gpsimd.tensor_tensor(panel(part, r), panel(part, r), sum_buf(e),
                                        ALU.add).then_inc(part_added, 1)

            def split_lo(x):
                for n, k, by, _ in x.numbers:
                    if by != "pool":
                        continue
                    pool.wait_ge(hi_ready, n + 1)
                    x.wait_lo(pool)
                    nc.gpsimd.tensor_tensor(x.lo(k), x.src[:, k * W:(k + 1) * W],
                                            hi[:, n % HI_BUFS, :].bitcast(F32), ALU.subtract).then_inc(lo_by_pool, 1)

            for st in steps[:-1]:
                t, w = st.t, st.width
                if is_split(st):
                    for x in step_items(st):
                        if x is split_items[0]:
                            split_lo(x)
                        if next_item(x):
                            split_lo(next_item(x))
                        if x.sum is not None:
                            add_sums(x.sum, x.sum, x.row)
                        if x.held_sum is not None:
                            add_sums(x.held_sum, x.held_sum, t + 1)
                        if x.again == st.row_after:
                            pool.wait_ge(pow_asked, t + 2)
                            nc.gpsimd.tensor_tensor(rs[:, 4, :], rs[:, 2, :], neg_half[:, :],
                                                    ALU.pow).then_inc(pow_done, 1)
                    continue

                def pair(s, base, i):
                    e, eb = st.pair_sum(s, base), st.pair_sum(base, base)
                    add_sums(e, eb, t + 1)
                    if t >= 0:
                        add_sums(e + 1, eb + 1, s + (t + 1))
                    if 0 <= base - st.lag < st.early:
                        add_sums(e + w, eb + w, t + 1)

                def power():
                    pool.wait_ge(pow_asked, t + 2)
                    nc.gpsimd.tensor_tensor(rs[:, 4, :], rs[:, 2, :], neg_half[:, :],
                                            ALU.pow).then_inc(pow_done, 1)

                repeat(pool, st.pairs, 2, pair, apart=min(st.pairs, st.lag + st.early))
                for s in range(st.tail):
                    e = st.tail_sum(s)
                    if s >= st.early:
                        add_sums(e, e, t + 1)
                        e += 1
                    if t >= 0:
                        add_sums(e, e, t + 1 + st.pairs + s)
                    if st.row_early and s == ROW_AT:
                        power()
                if not st.row_early:
                    power()

            def norm_scales(e):
                b = e % 2
                pool.wait_ge(stats_done, e + 1)
                if e >= 2:
                    wait_normed(pool, e - 2)
                nc.gpsimd.tensor_scalar(nmean[:, b, :], mv[:, b, :, 0], -1.0, None, ALU.mult)
                link(nc.gpsimd.tensor_scalar(var_eps[:, b, :], mv[:, b, :, 1], EPS, None, ALU.add))
                link(nc.gpsimd.tensor_tensor(rstd[:, b, :], var_eps[:, b, :], neg_half[:, :], ALU.pow))
                nc.gpsimd.tensor_tensor(shift[:, b, :], nmean[:, b, :], rstd[:, b, :],
                                        ALU.mult).then_inc(norm_ready, 1)

            held_items = step_items(final)[:len(final.held)]
            split_lo(held_items[1])
            pool.wait_ge(scales_ready, 1)
            for e in range(NP + OWN_LEAD):
                if e < NP:
                    r = epilogue_rows()[e]
                    pool.wait_ge(xe_loaded[e // XGROUP], 16)
                    ox = own_x(e).rearrange("p (k d) -> p k d", k=K)
                    nc.gpsimd.tensor_tensor(ox, ox, own[:, r * K:(r + 1) * K].unsqueeze(2).to_broadcast([P, K, D]),
                                            ALU.mult).then_inc(own_scaled, 1)
                if e + 2 < len(held_items):
                    split_lo(held_items[e + 2])
                if e >= OWN_LEAD:
                    norm_scales(e - OWN_LEAD)

        @block.scalar
        def _(act):
            def load_held(st, s):
                t, r = st.t, st.t + 1
                c = LAST - st.pairs - s
                d = c - r
                if t >= d:
                    act.wait_ge(multiplied, st.held_prod[st.held.index(t - d)] + 1)
                if r >= 1:
                    wait_held(act, r - 1, r - 1 + d)
                act.dma_start(held_slot(r, c), adj_block(c, r)).then_inc(held_loaded[d], 16)

            def load_x_of(r):
                if r >= 2:
                    act.wait_ge(y_ready, r - 1)
                act.dma_start(xin[:, r % 2, :], x_rows[r * P:(r + 1) * P, :]).then_inc(x_loaded[r % 2], 16)

            def split_hi(x):
                x.wait(act)
                for n, k, _, _ in x.numbers:
                    if n < HI_BUFS:
                        act.wait_ge(row_summed, first_split + 1)
                    else:
                        wait_slice_used(act, n - HI_BUFS)
                    nc.scalar.activation(hi[:, n % HI_BUFS, :], x.src[:, k * W:(k + 1) * W],
                                         ACT.Copy).then_inc(hi_ready, 1)

            for st in steps[:-1]:
                if is_split(st):
                    load_x_of(st.t + 1)
                    for x in step_items(st):
                        split_hi(x)
                        s = x.j - HELD_AFTER - (len(st.held) - st.tail)
                        if x.j - HELD_AFTER < len(st.held) and 0 <= s < st.tail:
                            load_held(st, s)
                else:
                    for s in range(st.tail):
                        load_held(st, s)
                    load_x_of(st.t + 1)

            def normalise(f):
                m0, b, o = f % MIXED * W, f % 2, f % OUTS
                act.wait_ge(norm_ready, f + 1)
                if f == 0:
                    act.wait_ge(multiplied, final.prod_pairs)
                if f >= OUTS:
                    act.wait_ge(stored[o], f // OUTS * 16)
                for k in range(K):
                    ins = nc.scalar.activation(result(f)[:, k * D:(k + 1) * D],
                                               mixed[:, m0 + k * D:m0 + (k + 1) * D], ACT.Identity,
                                               bias=shift[:, b, k:k + 1], scale=rstd[:, b, k:k + 1])
                ins.then_inc(normed_by_act, 1)
                r = epilogue_rows()[f]
                wait_normed(act, f)
                act.dma_start(out_rows[r * P:(r + 1) * P, :], result(f)).then_inc(stored[o], 16)

            items = step_items(final)
            ahead = len(final.held) + 1
            act.wait_ge(multiplied, steps[-2].prod_pairs)
            for g in range(NP // XGROUP):
                r = epilogue_rows()[g * XGROUP]
                act.dma_start(x_groups[g].rearrange("p (r f) -> p r f", f=W),
                              x_rows[r * P:(r + XGROUP) * P, :].rearrange("(r p) f -> p r f", p=P)
                              ).then_inc(xe_loaded[g], 16)
            for x in items[:ahead]:
                split_hi(x)
            act.wait_ge(scales_ready, 1)
            for e in range(NP):
                r, b = epilogue_rows()[e], e % 2
                act.wait_ge(transposed, e + 1)
                m0 = e % MIXED * W
                if e >= MIXED:
                    act.wait_ge(normed_by_act, e - MIXED + 1)
                for k in range(K):
                    ins = nc.scalar.activation(mixed[:, m0 + k * D:m0 + (k + 1) * D],
                                               turned[:, b, k * P:(k + 1) * P], ACT.Copy,
                                               scale=nbr[:, r * K + k:r * K + k + 1])
                ins.then_inc(nbr_scaled, 1)
                if e + ahead < NP:
                    split_hi(items[e + ahead])
                if 2 <= e < NP - BY_DVE:
                    normalise(e - 2)
            for f in range(NP - BY_DVE - 2, NP - BY_DVE):
                normalise(f)


def kernel(x, adj, L0_gnn_lambda_):
    import numpy as np
    import concourse.bacc as bacc
    from concourse.bass_utils import run_bass_kernel_spmd

    x, adj, lam = np.asarray(x), np.asarray(adj), np.asarray(L0_gnn_lambda_)
    NP = x.shape[0] // W
    blocks = adj.reshape(NP, W, NP, P, K).transpose(2, 0, 3, 4, 1).reshape(NP, NP, P, K * W)
    arrays = {"x_dram": np.ascontiguousarray(x), "adj_dram": np.ascontiguousarray(blocks),
              "lam_dram": np.ascontiguousarray(lam.reshape(1, 1))}
    nc = bacc.Bacc("TRN2", target_bir_lowering=False, num_devices=1)
    args = [nc.dram_tensor(n, a.shape, mybir.dt.from_np(a.dtype), kind="ExternalInput").ap()
            for n, a in arrays.items()]
    out = nc.dram_tensor("out_dram", x.shape, F32, kind="ExternalOutput").ap()
    gnn_resnorm(nc, *args, out)
    r = run_bass_kernel_spmd(nc, [arrays], core_ids=[0])
    return r.results[0]["out_dram"]
```
